# Optimizing a Trainium2 kernel written in Bass

```python
import numpy as np
import jax
import jax.numpy as jnp

def _softmax(x, axis=-1):
    return jax.nn.softmax(x, axis=axis)

def _gelu(x):
    return jax.nn.gelu(x, approximate=True)

def _silu(x):
    return jax.nn.silu(x)

def _sigmoid(x):
    return jax.nn.sigmoid(x)

def _layernorm(x, axis=-1, eps=1e-05):
    m = jnp.mean(x, axis=axis, keepdims=True)
    v = jnp.var(x, axis=axis, keepdims=True)
    return (x - m) / jnp.sqrt(v + eps)

def _scatter_add(tgt, idx, src, axis=0):
    return tgt.at[idx].add(src)

def _segment_sum(src, seg, n):
    return jax.ops.segment_sum(src, seg, n)
kernel_name = 'mk_pixart_seq_d2_seqx_r8_b7dfe6'

def setup_inputs(seed: int=0):
    np.random.seed(seed)
    _w = jnp.asarray

    def _rec_inputs():
        import jax
        import jax.numpy as jnp
        _rk = jax.random.key(seed)
        x = -0.0003929 + 0.9999 * jax.random.normal(jax.random.fold_in(_rk, 1), (16, 128, 128), jnp.float32)
        _lenS = 128 - jax.random.randint(jax.random.fold_in(_rk, 7), (16,), 0, max(1, 128 // 4) + 1, jnp.int32)
        _lenS2 = 128 - jax.random.randint(jax.random.fold_in(_rk, 8), (16,), 0, max(1, 128 // 4) + 1, jnp.int32)
        _ctx_1024P = jax.random.normal(jax.random.fold_in(_rk, 11), (16, 16, 128), jnp.float32)
        _ctx_1024c = jax.random.dirichlet(jax.random.fold_in(_rk, 511), 0.3 * jnp.ones((16,), jnp.float32), (16, 128))
        _ctx_1024t = jnp.einsum('bsk,bkd->bsd', _ctx_1024c, _ctx_1024P)
        _ctx_1024t = _ctx_1024t * jax.lax.rsqrt(jnp.mean(jnp.square(_ctx_1024t)) + 1e-12) * 0.953939
        ctx_1024 = -1.39393e-06 + 0.999914 * (_ctx_1024t + 0.3 * jax.random.normal(jax.random.fold_in(_rk, 611), (16, 128, 128), jnp.float32))
        cond_1024 = -0.00920427 + 1.00102 * jax.random.normal(jax.random.fold_in(_rk, 12), (16, 128), jnp.float32)
        return (x, ctx_1024, cond_1024)
    x, ctx_1024, cond_1024 = _rec_inputs()

    def _L0_xcond_setup():
        import jax, jax.numpy as jnp
        import numpy as np
        EPS = 1e-05

        def _ada_ln(x, c, W_ss, b_ss):
            mu = jnp.mean(x, axis=-1, keepdims=True)
            var = jnp.mean((x - mu) ** 2, axis=-1, keepdims=True)
            h = (x - mu) / jnp.sqrt(var + EPS)
            ss = jax.nn.silu(c) @ W_ss + b_ss
            scale, bias = jnp.split(ss, 2, axis=-1)
            return (1.0 + scale)[:, None, :] * h + bias[:, None, :]
        key = jax.random.key(seed)
        ks = jax.random.split(key, 12)
        B, Lq, Lkv, H = (8, 256, 64, 128)
        s = 0.02
        return {'x_q': jax.random.normal(ks[0], (B, Lq, H), jnp.float32), 'x_kv': jax.random.normal(ks[1], (B, Lkv, H), jnp.float32), 't_vec': jax.random.normal(ks[2], (B, H), jnp.float32), 'Wq': jax.random.normal(ks[3], (H, H), jnp.float32) * s, 'bq': jnp.zeros((H,), jnp.float32), 'Wkv': jax.random.normal(ks[4], (H, 2 * H), jnp.float32) * s, 'bkv': jnp.zeros((2 * H,), jnp.float32), 'Wp': jax.random.normal(ks[5], (H, H), jnp.float32) * s, 'bp': jnp.zeros((H,), jnp.float32), 'Wss_q': jax.random.normal(ks[6], (H, 2 * H), jnp.float32) * s, 'bss_q': jnp.zeros((2 * H,), jnp.float32), 'Wss_kv': jax.random.normal(ks[7], (H, 2 * H), jnp.float32) * s, 'bss_kv': jnp.zeros((2 * H,), jnp.float32)}
    _L0_xcond_all = _L0_xcond_setup()
    _L0_xcond_in = {k: v for k, v in _L0_xcond_all.items() if k in ('Wq', 'bq', 'Wkv', 'bkv', 'Wp', 'bp', 'Wss_q', 'bss_q', 'Wss_kv', 'bss_kv')}
    del _L0_xcond_all

    def _L1_xcond_setup():
        import jax, jax.numpy as jnp
        import numpy as np
        LN_EPS = 1e-06

        def _ln(x):
            mu = jnp.mean(x, axis=-1, keepdims=True)
            var = jnp.var(x, axis=-1, keepdims=True)
            return (x - mu) * jax.lax.rsqrt(var + LN_EPS)
        key = jax.random.key(seed)
        H, NH = (128, 16)
        B, N, S = (4, 128, 77)
        MLP = int(H * 4.0)
        ks = jax.random.split(key, 20)
        s = 1.0 / np.sqrt(H)
        return {'x': jax.random.normal(ks[0], (B, N, H), jnp.float32), 'c': jax.random.normal(ks[1], (B, H), jnp.float32), 'context': jax.random.normal(ks[2], (B, S, H), jnp.float32), 'W_mod': jax.random.normal(ks[3], (H, 6 * H), jnp.float32) * s, 'b_mod': jnp.zeros((6 * H,), jnp.float32), 'W_qkv': jax.random.normal(ks[4], (H, 3 * H), jnp.float32) * s, 'b_qkv': jnp.zeros((3 * H,), jnp.float32), 'W_proj': jax.random.normal(ks[5], (H, H), jnp.float32) * s, 'b_proj': jnp.zeros((H,), jnp.float32), 'W_qc': jax.random.normal(ks[6], (H, H), jnp.float32) * s, 'b_qc': jnp.zeros((H,), jnp.float32), 'W_kvc': jax.random.normal(ks[7], (H, 2 * H), jnp.float32) * s, 'b_kvc': jnp.zeros((2 * H,), jnp.float32), 'W_cproj': jax.random.normal(ks[8], (H, H), jnp.float32) * s, 'b_cproj': jnp.zeros((H,), jnp.float32), 'W_mlp1': jax.random.normal(ks[9], (H, MLP), jnp.float32) * s, 'b_mlp1': jnp.zeros((MLP,), jnp.float32), 'W_mlp2': jax.random.normal(ks[10], (MLP, H), jnp.float32) * (1.0 / np.sqrt(MLP)), 'b_mlp2': jnp.zeros((H,), jnp.float32)}
    _L1_xcond_all = _L1_xcond_setup()
    _L1_xcond_in = {k: v for k, v in _L1_xcond_all.items() if k in ('W_mod', 'b_mod', 'W_qkv', 'b_qkv', 'W_proj', 'b_proj', 'W_qc', 'b_qc', 'W_kvc', 'b_kvc', 'W_cproj', 'b_cproj', 'W_mlp1', 'b_mlp1', 'W_mlp2', 'b_mlp2')}
    del _L1_xcond_all
    return {'x': x, 'ctx_1024': ctx_1024, 'cond_1024': cond_1024, 'L0_xcond_Wq': _L0_xcond_in['Wq'], 'L0_xcond_bq': _L0_xcond_in['bq'], 'L0_xcond_Wkv': _L0_xcond_in['Wkv'], 'L0_xcond_bkv': _L0_xcond_in['bkv'], 'L0_xcond_Wp': _L0_xcond_in['Wp'], 'L0_xcond_bp': _L0_xcond_in['bp'], 'L0_xcond_Wss_q': _L0_xcond_in['Wss_q'], 'L0_xcond_bss_q': _L0_xcond_in['bss_q'], 'L0_xcond_Wss_kv': _L0_xcond_in['Wss_kv'], 'L0_xcond_bss_kv': _L0_xcond_in['bss_kv'], 'L1_xcond_W_mod': _L1_xcond_in['W_mod'], 'L1_xcond_b_mod': _L1_xcond_in['b_mod'], 'L1_xcond_W_qkv': _L1_xcond_in['W_qkv'], 'L1_xcond_b_qkv': _L1_xcond_in['b_qkv'], 'L1_xcond_W_proj': _L1_xcond_in['W_proj'], 'L1_xcond_b_proj': _L1_xcond_in['b_proj'], 'L1_xcond_W_qc': _L1_xcond_in['W_qc'], 'L1_xcond_b_qc': _L1_xcond_in['b_qc'], 'L1_xcond_W_kvc': _L1_xcond_in['W_kvc'], 'L1_xcond_b_kvc': _L1_xcond_in['b_kvc'], 'L1_xcond_W_cproj': _L1_xcond_in['W_cproj'], 'L1_xcond_b_cproj': _L1_xcond_in['b_cproj'], 'L1_xcond_W_mlp1': _L1_xcond_in['W_mlp1'], 'L1_xcond_b_mlp1': _L1_xcond_in['b_mlp1'], 'L1_xcond_W_mlp2': _L1_xcond_in['W_mlp2'], 'L1_xcond_b_mlp2': _L1_xcond_in['b_mlp2']}

def reference(x, ctx_1024, cond_1024, L0_xcond_Wq, L0_xcond_bq, L0_xcond_Wkv, L0_xcond_bkv, L0_xcond_Wp, L0_xcond_bp, L0_xcond_Wss_q, L0_xcond_bss_q, L0_xcond_Wss_kv, L0_xcond_bss_kv, L1_xcond_W_mod, L1_xcond_b_mod, L1_xcond_W_qkv, L1_xcond_b_qkv, L1_xcond_W_proj, L1_xcond_b_proj, L1_xcond_W_qc, L1_xcond_b_qc, L1_xcond_W_kvc, L1_xcond_b_kvc, L1_xcond_W_cproj, L1_xcond_b_cproj, L1_xcond_W_mlp1, L1_xcond_b_mlp1, L1_xcond_W_mlp2, L1_xcond_b_mlp2):
    import jax
    import jax.numpy as jnp

    def _L0_xcond_ref(x_q, x_kv, t_vec, Wq, bq, Wkv, bkv, Wp, bp, Wss_q, bss_q, Wss_kv, bss_kv):
        import jax, jax.numpy as jnp
        import numpy as np
        EPS = 1e-05

        def _ada_ln(x, c, W_ss, b_ss):
            mu = jnp.mean(x, axis=-1, keepdims=True)
            var = jnp.mean((x - mu) ** 2, axis=-1, keepdims=True)
            h = (x - mu) / jnp.sqrt(var + EPS)
            ss = jax.nn.silu(c) @ W_ss + b_ss
            scale, bias = jnp.split(ss, 2, axis=-1)
            return (1.0 + scale)[:, None, :] * h + bias[:, None, :]
        B, Lq, H = x_q.shape
        Lkv = x_kv.shape[1]
        nh = 16
        dh = H // nh
        xq = _ada_ln(x_q, t_vec, Wss_q, bss_q)
        xkv = _ada_ln(x_kv, t_vec, Wss_kv, bss_kv)
        q = (xq @ Wq + bq).reshape(B, Lq, nh, dh)
        kv = (xkv @ Wkv + bkv).reshape(B, Lkv, 2, nh, dh)
        k = kv[:, :, 0]
        v = kv[:, :, 1]
        scores = jnp.einsum('bqhd,bkhd->bhqk', q, k) / jnp.sqrt(jnp.float32(dh))
        attn = jax.nn.softmax(scores, axis=-1)
        out = jnp.einsum('bhqk,bkhd->bqhd', attn, v).reshape(B, Lq, H)
        return x_q + (out @ Wp + bp)

    def _L1_xcond_ref(x, c, context, W_mod, b_mod, W_qkv, b_qkv, W_proj, b_proj, W_qc, b_qc, W_kvc, b_kvc, W_cproj, b_cproj, W_mlp1, b_mlp1, W_mlp2, b_mlp2):
        import jax, jax.numpy as jnp
        import numpy as np
        LN_EPS = 1e-06

        def _ln(x):
            mu = jnp.mean(x, axis=-1, keepdims=True)
            var = jnp.var(x, axis=-1, keepdims=True)
            return (x - mu) * jax.lax.rsqrt(var + LN_EPS)
        B, N, H = x.shape
        NH = 16
        hd = H // NH
        scale = hd ** (-0.5)
        c_proj = jax.nn.silu(c) @ W_mod + b_mod
        shift_a, scale_a, gate_a, shift_m, scale_m, gate_m = jnp.split(c_proj, 6, axis=-1)

        def modulate(t, shift, sc):
            return t * (1 + sc[:, None]) + shift[:, None]
        x_norm = modulate(_ln(x), shift_a, scale_a)
        qkv = x_norm @ W_qkv + b_qkv
        q, k, v = jnp.split(qkv, 3, axis=-1)
        q = q.reshape(B, N, NH, hd).transpose(0, 2, 1, 3)
        k = k.reshape(B, N, NH, hd).transpose(0, 2, 1, 3)
        v = v.reshape(B, N, NH, hd).transpose(0, 2, 1, 3)
        attn_w = jax.nn.softmax(jnp.einsum('bhqd,bhkd->bhqk', q, k) * scale, axis=-1)
        attn_out = jnp.einsum('bhqk,bhkd->bhqd', attn_w, v)
        attn_out = attn_out.transpose(0, 2, 1, 3).reshape(B, N, H)
        attn_out = attn_out @ W_proj + b_proj
        x = x + gate_a[:, None] * attn_out
        S = context.shape[1]
        q_c = _ln(x) @ W_qc + b_qc
        kv_c = _ln(context) @ W_kvc + b_kvc
        k_c, v_c = jnp.split(kv_c, 2, axis=-1)
        q_c = q_c.reshape(B, N, NH, hd).transpose(0, 2, 1, 3)
        k_c = k_c.reshape(B, S, NH, hd).transpose(0, 2, 1, 3)
        v_c = v_c.reshape(B, S, NH, hd).transpose(0, 2, 1, 3)
        c_attn_w = jax.nn.softmax(jnp.einsum('bhqd,bhsd->bhqs', q_c, k_c) * scale, axis=-1)
        c_attn_out = jnp.einsum('bhqs,bhsd->bhqd', c_attn_w, v_c)
        c_attn_out = c_attn_out.transpose(0, 2, 1, 3).reshape(B, N, H)
        c_attn_out = c_attn_out @ W_cproj + b_cproj
        x = x + c_attn_out
        x_norm2 = modulate(_ln(x), shift_m, scale_m)
        h = jax.nn.gelu(x_norm2 @ W_mlp1 + b_mlp1)
        h = h @ W_mlp2 + b_mlp2
        x = x + gate_m[:, None] * h
        return x
    x = _L0_xcond_ref(x, ctx_1024, cond_1024, L0_xcond_Wq, L0_xcond_bq, L0_xcond_Wkv, L0_xcond_bkv, L0_xcond_Wp, L0_xcond_bp, L0_xcond_Wss_q, L0_xcond_bss_q, L0_xcond_Wss_kv, L0_xcond_bss_kv)
    x = _L1_xcond_ref(x, cond_1024, ctx_1024, L1_xcond_W_mod, L1_xcond_b_mod, L1_xcond_W_qkv, L1_xcond_b_qkv, L1_xcond_W_proj, L1_xcond_b_proj, L1_xcond_W_qc, L1_xcond_b_qc, L1_xcond_W_kvc, L1_xcond_b_kvc, L1_xcond_W_cproj, L1_xcond_b_cproj, L1_xcond_W_mlp1, L1_xcond_b_mlp1, L1_xcond_W_mlp2, L1_xcond_b_mlp2)
    return x

_drawn_inputs = setup_inputs


def setup_inputs(seed=0):
    import zlib

    import numpy as np

    out = dict(_drawn_inputs(seed))
    spreads = {'L0_xcond_bq': (0.0, 2.0),
     'L0_xcond_bkv': (0.0, 0.345),
     'L0_xcond_bp': (0.0, 0.1),
     'L0_xcond_bss_q': (0.0, 2.0),
     'L0_xcond_bss_kv': (0.0, 0.8),
     'L1_xcond_b_mod': (0.0, 0.1),
     'L1_xcond_b_qkv': (0.0, 0.1),
     'L1_xcond_b_proj': (0.0, 0.1),
     'L1_xcond_b_qc': (0.0, 0.496),
     'L1_xcond_b_kvc': (0.0, 0.1),
     'L1_xcond_b_cproj': (0.0, 0.1),
     'L1_xcond_b_mlp1': (0.0, 0.1),
     'L1_xcond_b_mlp2': (0.0, 0.1)}
    factors = {'L0_xcond_Wq': 8.0, 'L0_xcond_Wss_q': 27.416, 'L0_xcond_Wss_kv': 7.002}
    for name, (base, spread) in spreads.items():
        noise = np.random.default_rng([zlib.crc32(name.encode()), seed]).standard_normal(out[name].shape)
        drawn = base * np.exp(spread * noise) if base else spread * noise
        out[name] = jnp.asarray(drawn.astype(out[name].dtype))
    for name, factor in factors.items():
        out[name] = (out[name] * factor).astype(out[name].dtype)
    return out
```

```python
from contextlib import ExitStack

import concourse.bass as bass
from concourse import mybir

F32 = mybir.dt.float32
BF16 = mybir.dt.bfloat16
U32 = mybir.dt.uint32
ALU = mybir.AluOpType
ACT = mybir.ActivationFunctionType
AX = mybir.AxisListType

CROSS0, SELF1, CROSS1 = range(3)
LAYERS = 3
EPS = (1e-5, 1e-6, 1e-6, 1e-6)

B, T, H = 16, 128, 128
HEADS = 16
D = H // HEADS
PAIRS = HEADS // 2
HALF = 64
MLP = 4
UNITS = LAYERS * B
PER = 4
GROUPS = UNITS // PER
MLP_GROUPS = B // PER
TOK = PER * T
CHUNK = HEADS // 2
CP = CHUNK // 2

Q_PART = (0, 0, 0, 1, 1, 2)
K_PART = (0, 1, 2, 0, 1, 0)
TERMS = len(Q_PART)
SROWS = TERMS * D
MROWS = SROWS + 2
STACKS = 3
MOVES = 2 * TERMS
QUAD = 32
MISC = 3

R_Q, R_K, R_V = (0, 3, 6), (1, 4, 7), (2, 5, 8)
R_SSQ, R_SSKV, R_MOD, R_MLP1, R_MLP2, ROWS = 9, 11, 13, 19, 23, 24
M_SCALE = (0, 5, None, 7)
M_SHIFT = (1, 4, None, 6)
M_KV_SCALE, M_KV_SHIFT = 2, 3


def build(nc, x, ctx_1024, cond_1024, L0_xcond_Wq, L0_xcond_bq, L0_xcond_Wkv, L0_xcond_bkv,
          L0_xcond_Wp, L0_xcond_bp, L0_xcond_Wss_q, L0_xcond_bss_q, L0_xcond_Wss_kv,
          L0_xcond_bss_kv, L1_xcond_W_mod, L1_xcond_b_mod, L1_xcond_W_qkv, L1_xcond_b_qkv,
          L1_xcond_W_proj, L1_xcond_b_proj, L1_xcond_W_qc, L1_xcond_b_qc, L1_xcond_W_kvc,
          L1_xcond_b_kvc, L1_xcond_W_cproj, L1_xcond_b_cproj, L1_xcond_W_mlp1, L1_xcond_b_mlp1,
          L1_xcond_W_mlp2, L1_xcond_b_mlp2, out):
    x_d = x.rearrange("b t h -> t b h")
    ctx_d = ctx_1024.rearrange("b t h -> t b h")
    out_d = out.rearrange("b t h -> t b h")

    def row(v):
        return v.rearrange("(r n) -> r n", n=H)

    with ExitStack() as stack:
        def sb(name, shape, dt=F32):
            return stack.enter_context(nc.sbuf_tensor(name, shape, dt))

        def sem(name):
            return stack.enter_context(nc.semaphore(name))

        score_ps = stack.enter_context(nc.psum_tensor("score_ps", [128, 2, 512], F32))
        keyed_ps = stack.enter_context(nc.psum_tensor("keyed_ps", [128, 2, 512], F32))
        attn_ps = stack.enter_context(nc.psum_tensor("attn_ps", [128, 512], F32))
        misc_ps = stack.enter_context(nc.psum_tensor("misc_ps", [128, MISC, 512], F32))

        xs = sb("xs", [T, B, H])
        cs = sb("cs", [T, B, H])
        wq0, wkv0, wp0 = sb("wq0", [H, H]), sb("wkv0", [H, 2 * H]), sb("wp0", [H, H])
        wssq, wsskv = sb("wssq", [H, 2 * H]), sb("wsskv", [H, 2 * H])
        wmod, wqkv, wproj = sb("wmod", [H, 6 * H]), sb("wqkv", [H, 3 * H]), sb("wproj", [H, H])
        wqc, wkvc, wcproj = sb("wqc", [H, H]), sb("wkvc", [H, 2 * H]), sb("wcproj", [H, H])
        w1, w2 = sb("w1", [H, MLP * H]), sb("w2", [H, MLP, H])
        w_qk = sb("w_qk", [H, LAYERS, 2, H])
        brow, brow_p = sb("brow", [ROWS, H]), sb("brow_p", [ROWS, H])
        bcol, bcol_p = sb("bcol", [H, ROWS]), sb("bcol_p", [H, ROWS])
        b_out = sb("b_out", [128, LAYERS, H])
        b_gate = sb("b_gate", [128, 2, H])
        c_raw, c_exp, c_sig = sb("c_raw", [B, H]), sb("c_exp", [B, H]), sb("c_sig", [B, H])
        c_silu = sb("c_silu", [B, H])
        c_col, c_rep = sb("c_col", [H, B]), sb("c_rep", [H, B, 128])
        mod = sb("mod", [H, 8, B])
        gate = sb("gate", [128, B, 2, H])
        ident, ident_b = sb("ident", [128, 128]), sb("ident_b", [128, 128], BF16)
        minus_half = sb("minus_half", [128, PER])
        stats = sb("stats", [T, 2, PER, 6])
        x_mv, c_mv = sb("x_mv", [T, PER, 2]), sb("c_mv", [T, B, 2])
        var_eps, rstd = sb("var_eps", [T, 2, PER]), sb("rstd", [T, 2, PER])
        normed = sb("normed", [T, 2, PER, H])
        normed_t = sb("normed_t", [H, 2, PER, T])
        parts = sb("parts", [128, 2, 3, TOK], BF16)
        rest = sb("rest", [128, 2, TOK])
        stack_q = sb("stack_q", [128, STACKS, PAIRS, TOK], BF16)
        stack_k = sb("stack_k", [128, STACKS, PAIRS, TOK], BF16)
        values = sb("values", [T, STACKS, PER, HEADS, QUAD])
        neg_max = sb("neg_max", [T, 2, 2, PAIRS])
        max_parts = sb("max_parts", [T, 2, 2, 2, PAIRS], BF16)
        max_rows = sb("max_rows", [2 * HEADS, 2, T], BF16)
        probs = sb("probs", [T, 3, CHUNK * T])
        summed = sb("summed", [128, 2, 4, T])
        r_sum = sb("r_sum", [T, 2, HEADS])
        attn = sb("attn", [T, 2, H])
        attn_t = sb("attn_t", [H, 2, T])
        x_bias = sb("x_bias", [T, 2, H])
        branch = sb("branch", [T, 2, H])
        mlp_in = c_rep
        hidden = sb("hidden", [H, 2, MLP, 4 * T])
        mlp_t, mlp_out = sb("mlp_t", [H, 2, 4 * T]), sb("mlp_out", [T, 2, 4 * H])

        loaded = {n: sem("loaded_" + n) for n in (
            "cond", "brow", "wss", "wmod", "wA", "wB", "wC", "w1", "w2", "bout")}
        x_in = [sem(f"x_in{i}") for i in range(4)]
        c_in = [sem(f"c_in{i}") for i in range(4)]
        consts_ready, stack_ones, values_ones = sem("consts_ready"), sem("stack_ones"), sem("values_ones")
        rows_permuted, w_permuted = sem("rows_permuted"), sem("w_permuted")
        cond_exp, cond_step, cond_rep = sem("cond_exp"), sem("cond_step"), sem("cond_rep")
        setup_ps, bias_cols, mod_ready = sem("setup_ps"), sem("bias_cols"), sem("mod_ready")
        gate_ps, gate_ready = sem("gate_ps"), sem("gate_ready")
        stat_step, rstd_ready, normed_ready = sem("stat_step"), sem("rstd_ready"), sem("normed_ready")
        normed_ps, normed_t_ready = sem("normed_ps"), sem("normed_t_ready")
        qk_ps, hi_ready, rest_ready, split_ready = sem("qk_ps"), sem("hi_ready"), sem("rest_ready"), sem("split_ready")
        v_ps, v_ready = sem("v_ps"), sem("v_ready")
        q_landed = [sem(f"q_landed{i}") for i in range(STACKS)]
        k_landed = [sem(f"k_landed{i}") for i in range(STACKS)]
        score_done, max_done, max_split, max_ps, max_row_ready = (
            sem("score_done"), sem("max_done"), sem("max_split"), sem("max_ps"), sem("max_row_ready"))
        max_landed = [sem(f"max_landed{i}") for i in range(4)]
        keyed_done, probs_ready, attn_done = sem("keyed_done"), sem("probs_ready"), sem("attn_done")
        summed_ready, turned_ps = sem("summed_ready"), sem("turned_ps")
        sum_inv, attn_ready, attn_t_ps, attn_t_ready = (
            sem("sum_inv"), sem("attn_ready"), sem("attn_t_ps"), sem("attn_t_ready"))
        proj_ps, branch_added, x_bias_ready, gated = (
            sem("proj_ps"), sem("branch_added"), sem("x_bias_ready"), sem("gated"))
        hidden_ps, hidden_ready, mlp_ps, mlp_t_ready, mlp_turned, mlp_gated = (
            sem("hidden_ps"), sem("hidden_ready"), sem("mlp_ps"), sem("mlp_t_ready"), sem("mlp_turned"), sem("mlp_gated"))
        x_final, stored = sem("x_final"), sem("stored")

        block = stack.enter_context(nc.Block())

        MLP_TICK = UNITS
        FIRST, LAST = -10, MLP_TICK + 6

        def unit(u):
            return 0 <= u < UNITS

        def front_at(tick, step):
            g, left = divmod(tick - step + 10, PER)
            return g if left == 0 and 0 <= g < GROUPS + MLP_GROUPS and (g < GROUPS or step < 2) else None

        def layer(g):
            return g // (B // PER)

        def batches(g):
            b = PER * (g % (B // PER))
            return b, b + PER

        NORMS = [(g, n) for g in range(GROUPS + MLP_GROUPS) for n in range(2)
                 if n == 0 or layer(g) in (CROSS0, CROSS1)]

        def norms_to(g, n):
            return NORMS.index((g, n)) + 1

        def stat_steps_to(g, n):
            return sum(1 if (layer(a), m) == (CROSS1, 1) else 2 * PER + 1 for a, m in NORMS[:norms_to(g, n)])

        def at_tick(tick):
            g1, g2, g3 = (front_at(tick, i) for i in (1, 2, 3))
            return ([("max", tick + 1)] * unit(tick + 1) + [("norm", g1, 0)] * (g1 is not None)
                    + [("norm", g2, 1)] * (g2 is not None and (g2, 1) in NORMS)
                    + [("k", g3)] * (g3 is not None) + [("proj", tick - 2)] * unit(tick - 2)
                    + [("out", tick - 1)] * unit(tick - 1) + [("gate", tick)] * (0 <= tick < B)
                    + [("q", g2)] * (g2 is not None) + [("v", g3)] * (g3 is not None)
                    + [("attn", tick - 1)] * unit(tick - 1)
                    + [("mlp", tick - MLP_TICK - 2)] * (0 <= tick - MLP_TICK - 2 < 4))

        MISC_ORDER = [("bias",), ("mod",)] + [use for tick in range(FIRST, LAST) for use in at_tick(tick)]
        read_by = {"bias": lambda: (bias_cols, 3), "mod": lambda: (mod_ready, 2),
                   "norm": lambda g, n: (normed_t_ready, norms_to(g, n)),
                   "q": lambda g: (rest_ready, 2 * g + 1), "k": lambda g: (rest_ready, 2 * g + 2),
                   "v": lambda g: (v_ready, g + 1), "gate": lambda b: (gate_ready, b + 1),
                   "out": lambda u: (attn_ready, u + 1), "mlp": lambda q: (mlp_gated, q + 1),
                   "attn": lambda u: (attn_t_ready, u + 1), "max": lambda u: (max_row_ready, u + 1),
                   "proj": lambda u: (branch_added, u + 1)}

        def misc(*use):
            return misc_ps[:, MISC_ORDER.index(use) % MISC, :]

        def q_in_place(eng, g):
            eng.wait_ge(q_landed[g % STACKS], 16 * MOVES * (g // STACKS + 1))

        def k_in_place(eng, g):
            eng.wait_ge(k_landed[g % STACKS], 16 * MOVES * (g // STACKS + 1))

        def max_rows_landed(eng, u):
            eng.wait_ge(max_landed[u % 4], 32 * (u // 4 + 1))

        @block.sync
        def _(sp):
            for i in range(4):
                sp.dma_start(xs[:, 4 * i:4 * i + 4, :], x_d[:, 4 * i:4 * i + 4, :]).then_inc(x_in[i], 16)
                sp.dma_start(cs[:, 4 * i:4 * i + 4, :], ctx_d[:, 4 * i:4 * i + 4, :]).then_inc(c_in[i], 16)
                if i == 0:
                    sp.dma_start(wq0[:, :], L0_xcond_Wq).then_inc(loaded["wA"], 16)
                    sp.dma_start(wkv0[:, :], L0_xcond_Wkv).then_inc(loaded["wA"], 16)
                    sp.dma_start(wp0[:, :], L0_xcond_Wp).then_inc(loaded["wA"], 16)
            sp.dma_start(wqkv[:, :], L1_xcond_W_qkv).then_inc(loaded["wB"], 16)
            sp.dma_start(wproj[:, :], L1_xcond_W_proj).then_inc(loaded["wB"], 16)
            sp.dma_start(wqc[:, :], L1_xcond_W_qc).then_inc(loaded["wC"], 16)
            sp.dma_start(wkvc[:, :], L1_xcond_W_kvc).then_inc(loaded["wC"], 16)
            sp.dma_start(wcproj[:, :], L1_xcond_W_cproj).then_inc(loaded["wC"], 16)
            sp.dma_start(w1[:, :], L1_xcond_W_mlp1).then_inc(loaded["w1"], 16)
            sp.dma_start(w2[:, :, :], L1_xcond_W_mlp2.rearrange("(c p) n -> p c n", p=H)).then_inc(loaded["w2"], 16)

            def move_parts(g, n, parity):
                if parity == 0:
                    sp.wait_ge(hi_ready, 2 * g + n + 1)
                    sp.wait_ge(split_ready, 2 * (2 * g + n + 1))
                    if n == 1:
                        sp.wait_ge(stack_ones, min(g, STACKS - 1) + 1)
                    if g >= STACKS:
                        sp.wait_ge(keyed_done, 2 * PER * (g - STACKS + 1))
                at = HALF * parity
                dst, part, landed = ((stack_q, Q_PART, q_landed), (stack_k, K_PART, k_landed))[n]
                for t in range(TERMS):
                    sp.dma_start(dst[at + D * t:at + D * (t + 1), g % STACKS, :, :],
                                 parts[at:at + HALF, n, part[t], :]).then_inc(landed[g % STACKS], 16)

            def move_max(u):
                sp.wait_ge(max_row_ready, u + 1)
                if u >= PER * STACKS:
                    sp.wait_ge(keyed_done, 2 * (u - PER * STACKS) + 2)
                j = u % PER
                for e in range(2):
                    sp.dma_start(stack_q[HALF * e + SROWS:HALF * e + MROWS, u // PER % STACKS, :, T * j:T * (j + 1)],
                                 max_rows[2 * PAIRS * e:2 * PAIRS * (e + 1), u % 2, :]).then_inc(max_landed[u % 4], 16)

            for tick in range(FIRST, LAST):
                if unit(tick + 1):
                    move_max(tick + 1)
                for step in (3, 4, 5, 6):
                    if front_at(tick, step) is not None:
                        move_parts(front_at(tick, step), (step - 3) // 2, (step - 3) % 2)
            for q in range(4):
                sp.wait_ge(x_final, q + 1)
                sp.dma_start(out_d[:, 4 * q:4 * q + 4, :], xs[:, 4 * q:4 * q + 4, :]).then_inc(stored, 16)
            sp.wait_ge(stored, 16 * 4)

        @block.tensor
        def _(pe):
            misc_taken = [0]

            def take_misc(*use):
                n = misc_taken[0]
                assert MISC_ORDER[n] == use
                if n >= MISC:
                    kind, *which = MISC_ORDER[n - MISC]
                    pe.wait_ge(*read_by[kind](*which))
                misc_taken[0] += 1
                return misc(*use)

            def setup():
                pe.wait_ge(consts_ready, 4)
                pe.wait_ge(loaded["brow"], 16 * 10)
                pe.wait_ge(rows_permuted, 1)
                ps = take_misc("bias")
                pe.transpose(ps[:, 0:ROWS], brow[:, :], ident[0:ROWS, 0:ROWS])
                pe.transpose(ps[:, 32:32 + ROWS], brow_p[:, :], ident[0:ROWS, 0:ROWS])
                pe.wait_ge(cond_step, 3)
                pe.transpose(ps[:, 64:64 + B], c_silu[:, :], ident[0:B, 0:B]).then_inc(setup_ps, 1)
                pe.wait_ge(bias_cols, 3)
                pe.wait_ge(loaded["wss"], 32)
                ps = take_misc("mod")
                blocks = [wssq[:, 0:H], wssq[:, H:2 * H], wsskv[:, 0:H], wsskv[:, H:2 * H]]
                blocks += [wmod[:, i * H:(i + 1) * H] for i in (0, 1, 3, 4)]
                for m, w in enumerate(blocks):
                    if m == 4:
                        pe.wait_ge(loaded["wmod"], 16)
                    mm = pe.matmul(ps[:, B * m:B * (m + 1)], w, c_col[:, :], start=True, stop=True)
                mm.then_inc(setup_ps, 1)

            def gates(b):
                if b == 0:
                    pe.wait_ge(cond_rep, 1)
                ps = take_misc("gate", b)
                w = wmod[:, :].rearrange("k (a n) -> k a n", n=H)[:, 2:6:3, :]
                pe.matmul(ps[:, 0:2 * H], c_rep[:, b, :], w, start=True, stop=True).then_inc(gate_ps, 1)

            def transpose_normed(g, n):
                pe.wait_ge(normed_ready, norms_to(g, n))
                ps = take_misc("norm", g, n)
                for j in range(PER):
                    mm = pe.transpose(ps[:, j * T:(j + 1) * T], normed[:, n, j, :], ident[:, :])
                mm.then_inc(normed_ps, 1)

            def project_qk(g, n):
                s = layer(g)
                src = 0 if s == SELF1 else n
                pe.wait_ge(normed_t_ready, norms_to(g, src))
                if g % (B // PER) == 0:
                    pe.wait_ge(w_permuted, 2 * (s + 1))
                pe.matmul(take_misc("qk"[n], g), w_qk[:, s, n, :], normed_t[:, src, :, :],
                          start=True, stop=True).then_inc(qk_ps, 1)

            def project_v(g):
                s = layer(g)
                w = (wkv0[:, H:2 * H], wqkv[:, 2 * H:3 * H], wkvc[:, H:2 * H])[s]
                ps = take_misc("v", g)
                for j in range(PER):
                    mm = pe.matmul(ps[:, j * H:(j + 1) * H], normed_t[:, 0 if s == SELF1 else 1, j, :],
                                   w, start=True, stop=True)
                mm.then_inc(v_ps, 1)

            def scores(u, c):
                g, j, n = u // PER, u % PER, 2 * u + c
                if c == 0 and j == 0:
                    q_in_place(pe, g)
                    k_in_place(pe, g)
                if n >= 1:
                    pe.wait_ge(max_done, n)
                cols = slice(T * j, T * (j + 1))
                for a in range(CP):
                    for e in range(2):
                        rows = slice(HALF * e, HALF * e + SROWS)
                        mm = pe.matmul(score_ps[:, e, a * T:(a + 1) * T],
                                       stack_q[rows, g % STACKS, CP * c + a, cols],
                                       stack_k[rows, g % STACKS, CP * c + a, cols], start=True, stop=True)
                mm.then_inc(score_done, 1)

            def turn_max(u):
                pe.wait_ge(max_split, 2 * (u + 1))
                ps = take_misc("max", u)
                pe.transpose(ps[0:2 * HEADS, 0:T // 2].bitcast(BF16),
                             max_parts[:, u % 2, :, :, :].rearrange("t e i p -> t (e i p)"),
                             ident_b[:, :]).then_inc(max_ps, 1)

            def keyed_scores(u, c):
                g, j, n = u // PER, u % PER, 2 * u + c
                if c == 0:
                    max_rows_landed(pe, u)
                if n >= 1:
                    pe.wait_ge(probs_ready, n)
                cols = slice(T * j, T * (j + 1))
                for a in range(CP):
                    for e in range(2):
                        rows = slice(HALF * e, HALF * e + MROWS)
                        mm = pe.matmul(keyed_ps[:, e, a * T:(a + 1) * T],
                                       stack_k[rows, g % STACKS, CP * c + a, cols],
                                       stack_q[rows, g % STACKS, CP * c + a, cols], start=True, stop=True)
                mm.then_inc(keyed_done, 1)

            def attend(u, c):
                n = 2 * u + c
                if c == 0 and u % PER == 0:
                    pe.wait_ge(v_ready, u // PER + 1)
                    if u < PER * STACKS:
                        pe.wait_ge(values_ones, 2)
                pe.wait_ge(probs_ready, n + 1)
                if c == 0 and u >= 1:
                    pe.wait_ge(summed_ready, u)
                for a in range(CP):
                    for e in range(2):
                        h = 2 * (CP * c + a) + e
                        at, slot = QUAD * (h % 4), h // 4
                        mm = pe.matmul(attn_ps[at:at + QUAD, slot * T:(slot + 1) * T],
                                       values[:, u // PER % STACKS, u % PER, h, :],
                                       probs[:, n % 3, (CP * e + a) * T:(CP * e + a + 1) * T], start=True, stop=True)
                mm.then_inc(attn_done, 1)

            def turn_summed(u):
                pe.wait_ge(summed_ready, u + 1)
                ps = take_misc("out", u)
                for i in range(4):
                    mm = pe.transpose(ps[:, i * 128:(i + 1) * 128], summed[:, u % 2, i, :], ident[:, :])
                mm.then_inc(turned_ps, 1)

            def turn_attn(u):
                pe.wait_ge(attn_ready, u + 1)
                pe.transpose(take_misc("attn", u)[:, 0:T], attn[:, u % 2, :], ident[:, :]).then_inc(attn_t_ps, 1)

            def project_out(u):
                w = (wp0, wproj, wcproj)[u // B]
                if u % B == 0:
                    pe.wait_ge(loaded[("wA", "wB", "wC")[u // B]], (48, 32, 48)[u // B])
                pe.wait_ge(attn_t_ready, u + 1)
                pe.matmul(take_misc("proj", u)[:, 0:H], attn_t[:, u % 2, :], w[:, :], start=True, stop=True).then_inc(proj_ps, 1)

            def mlp_up(q, c):
                if (q, c) == (0, 0):
                    pe.wait_ge(loaded["w1"], 16)
                if c == 0:
                    pe.wait_ge(normed_t_ready, norms_to(GROUPS + q, 0))
                n = MLP * q + c
                if n >= 2:
                    pe.wait_ge(hidden_ready, n - 1)
                else:
                    pe.wait_ge(probs_ready, 2 * UNITS)
                pe.matmul(keyed_ps[:, n % 2, :], w1[:, c * H:(c + 1) * H],
                          mlp_in[:, 4 * q:4 * q + 4, :], start=True, stop=True).then_inc(hidden_ps, 1)

            def mlp_down(q, c):
                if (q, c) == (0, 0):
                    pe.wait_ge(loaded["w2"], 16)
                pe.wait_ge(hidden_ready, MLP * q + c + 1)
                if c == 0 and q >= 2:
                    pe.wait_ge(mlp_t_ready, q - 1)
                mm = pe.matmul(score_ps[:, q % 2, :], w2[:, c, :], hidden[:, q % 2, c, :],
                               start=(c == 0), stop=(c == MLP - 1))
                if c == MLP - 1:
                    mm.then_inc(mlp_ps, 1)

            def turn_mlp(q):
                pe.wait_ge(mlp_t_ready, q + 1)
                ps = take_misc("mlp", q)
                for j in range(4):
                    mm = pe.transpose(ps[:, j * H:(j + 1) * H], mlp_t[:, q % 2, j * T:(j + 1) * T], ident[:, :])
                mm.then_inc(mlp_turned, 1)

            setup()
            for tick in range(FIRST, LAST):
                g1, g2, g3 = (front_at(tick, i) for i in (1, 2, 3))
                if unit(tick):
                    keyed_scores(tick, 0)
                if unit(tick + 2):
                    scores(tick + 2, 0)
                if unit(tick - 1):
                    attend(tick - 1, 1)
                if unit(tick + 1):
                    turn_max(tick + 1)
                if g1 is not None:
                    transpose_normed(g1, 0)
                if g2 is not None and (g2, 1) in NORMS:
                    transpose_normed(g2, 1)
                if g3 is not None:
                    project_qk(g3, 1)
                if unit(tick - 2):
                    project_out(tick - 2)
                if unit(tick):
                    keyed_scores(tick, 1)
                if unit(tick - 1):
                    turn_summed(tick - 1)
                if unit(tick + 2):
                    scores(tick + 2, 1)
                if 0 <= tick < B:
                    gates(tick)
                if g2 is not None:
                    project_qk(g2, 0)
                if g3 is not None:
                    project_v(g3)
                if unit(tick):
                    attend(tick, 0)
                if unit(tick - 1):
                    turn_attn(tick - 1)
                q = tick - MLP_TICK
                for c in range(MLP):
                    if 0 <= q < 4:
                        mlp_up(q, c)
                    if 0 <= q - 1 < 4:
                        mlp_down(q - 1, c)
                if 0 <= q - 2 < 4:
                    turn_mlp(q - 2)

        @block.scalar
        def _(act):
            act.dma_start(c_raw[:, :], cond_1024).then_inc(loaded["cond"], 16)
            act.dma_start(wssq[:, :], L0_xcond_Wss_q).then_inc(loaded["wss"], 16)
            act.dma_start(wsskv[:, :], L0_xcond_Wss_kv).then_inc(loaded["wss"], 16)
            for r, b in ((R_Q[0], L0_xcond_bq), (R_K[0], L0_xcond_bkv), (R_Q[1], L1_xcond_b_qkv),
                         (R_Q[2], L1_xcond_b_qc), (R_K[2], L1_xcond_b_kvc), (R_SSQ, L0_xcond_bss_q),
                         (R_SSKV, L0_xcond_bss_kv), (R_MOD, L1_xcond_b_mod), (R_MLP1, L1_xcond_b_mlp1),
                         (R_MLP2, L1_xcond_b_mlp2)):
                act.dma_start(brow[r:r + b.shape[0] // H, :], row(b)).then_inc(loaded["brow"], 16)
            act.wait_ge(loaded["cond"], 16)
            act.activation(c_exp[:, :], c_raw[:, :], ACT.Exp, scale=-1.0).then_inc(cond_exp, 1)
            act.dma_start(wmod[:, :], L1_xcond_W_mod).then_inc(loaded["wmod"], 16)
            for i, b in enumerate((L0_xcond_bp, L1_xcond_b_proj, L1_xcond_b_cproj)):
                act.dma_start(b_out[:, i, :], row(b).broadcast_to([128, H])).then_inc(loaded["bout"], 16)
            for i in range(2):
                r = 2 + 3 * i
                act.dma_start(b_gate[:, i, :], row(L1_xcond_b_mod)[r:r + 1, :].broadcast_to([128, H])).then_inc(loaded["bout"], 16)

            def modulate(g, n):
                s = layer(g)
                act.wait_ge(normed_ps, norms_to(g, n))
                if g >= 1 and s < LAYERS:
                    act.wait_ge(v_ps, g)
                    act.wait_ge(qk_ps, 2 * g)
                if g == 0:
                    act.wait_ge(mod_ready, 4)
                ps = misc("norm", g, n)
                if s == CROSS1:
                    act.activation(normed_t[:, n, :, :].rearrange("h j t -> h (j t)"), ps, ACT.Copy).then_inc(normed_t_ready, 1)
                    return
                scale, shift = (M_KV_SCALE, M_KV_SHIFT) if n else (M_SCALE[s], M_SHIFT[s])
                for j, b in enumerate(range(*batches(g))):
                    dst = mlp_in[:, b, :] if s == LAYERS else normed_t[:, n, j, :]
                    last = act.activation(dst, ps[:, j * T:(j + 1) * T], ACT.Identity,
                                          bias=mod[:, shift, b:b + 1], scale=mod[:, scale, b:b + 1])
                last.then_inc(normed_t_ready, 1)

            def first_part(g, n):
                s = layer(g)
                act.wait_ge(qk_ps, 2 * g + n + 1)
                if g >= 1:
                    (q_in_place, k_in_place)[n](act, g - 1)
                if g == 0:
                    act.wait_ge(bias_cols, 3)
                r = (R_Q, R_K)[n][s]
                act.activation(parts[:, n, 0, :], misc("qk"[n], g), ACT.Identity,
                               bias=bcol_p[:, r:r + 1]).then_inc(hi_ready, 1)

            def copy_values(g):
                act.wait_ge(v_ps, g + 1)
                if g == 0:
                    act.wait_ge(values_ones, 2)
                if g >= STACKS:
                    act.wait_ge(attn_done, 2 * PER * (g - STACKS + 1))
                act.activation(values[:, g % STACKS, :, :, 0:D],
                               misc("v", g).rearrange("t (j h d) -> t j h d", j=PER, d=D),
                               ACT.Copy).then_inc(v_ready, 1)

            def exponentials(u, c):
                n = 2 * u + c
                act.wait_ge(keyed_done, n + 1)
                if n >= 3:
                    act.wait_ge(attn_done, n - 2)
                act.activation(probs[:, n % 3, :], keyed_ps[:, :, :].rearrange("t e n -> t (e n)"),
                               ACT.Exp, scale=float(D) ** -0.5).then_inc(probs_ready, 1)

            def copy_summed(u):
                act.wait_ge(attn_done, 2 * u + 2)
                if u >= 2:
                    act.wait_ge(turned_ps, u - 1)
                act.activation(summed[:, u % 2, :, :].rearrange("p s t -> p (s t)"), attn_ps[:, :],
                               ACT.Copy).then_inc(summed_ready, 1)

            def attn_with_bias(u):
                act.wait_ge(attn_t_ps, u + 1)
                if u >= 2:
                    act.wait_ge(proj_ps, u - 1)
                r = R_V[u // B]
                act.activation(attn_t[:, u % 2, :], misc("attn", u)[:, 0:T], ACT.Identity,
                               bias=bcol[:, r:r + 1]).then_inc(attn_t_ready, 1)

            def activate_hidden(q, c):
                act.wait_ge(hidden_ps, MLP * q + c + 1)
                if q >= 2 and c == 0:
                    act.wait_ge(mlp_ps, q - 1)
                act.activation(hidden[:, q % 2, c, :], keyed_ps[:, c % 2, :], ACT.Gelu_apprx_tanh,
                               bias=bcol[:, R_MLP1 + c:R_MLP1 + c + 1]).then_inc(hidden_ready, 1)

            def mlp_out_bias(q):
                act.wait_ge(mlp_ps, q + 1)
                if q >= 2:
                    act.wait_ge(mlp_turned, q - 1)
                act.activation(mlp_t[:, q % 2, :], score_ps[:, q % 2, :], ACT.Identity,
                               bias=bcol[:, R_MLP2:R_MLP2 + 1]).then_inc(mlp_t_ready, 1)

            for tick in range(FIRST, LAST):
                g1, g2, g3 = (front_at(tick, i) for i in (1, 2, 3))
                if unit(tick):
                    exponentials(tick, 0)
                if unit(tick - 1):
                    copy_summed(tick - 1)
                if g1 is not None:
                    modulate(g1, 0)
                if g2 is not None and (g2, 1) in NORMS:
                    modulate(g2, 1)
                if g3 is not None:
                    first_part(g3, 1)
                if unit(tick):
                    exponentials(tick, 1)
                if g2 is not None:
                    first_part(g2, 0)
                if g3 is not None:
                    copy_values(g3)
                if unit(tick - 1):
                    attn_with_bias(tick - 1)
                q = tick - MLP_TICK
                for c in range(MLP):
                    if 0 <= q < 4:
                        activate_hidden(q, c)
                if 0 <= q - 1 < 4:
                    mlp_out_bias(q - 1)

        @block.vector
        def _(dve):
            stat_steps = [0]

            def stat(ins):
                ins.then_inc(stat_step, 1)
                stat_steps[0] += 1

            for i in range(STACKS):
                dve.memset(stack_k[:, i, :, :].rearrange("p a n -> p (a n)").bitcast(U32), 0x3F803F80).then_inc(stack_ones, 1)
            dve.wait_ge(cond_exp, 1)
            dve.tensor_scalar(c_sig[:, :], c_exp[:, :], 1.0, None, ALU.add).then_inc(cond_step, 1)
            dve.wait_ge(cond_step, 1)
            dve.reciprocal(c_exp[:, :], c_sig[:, :]).then_inc(cond_step, 1)
            dve.wait_ge(cond_step, 2)
            dve.tensor_tensor(c_silu[:, :], c_raw[:, :], c_exp[:, :], ALU.mult).then_inc(cond_step, 1)
            dve.wait_ge(setup_ps, 1)
            dve.tensor_copy(bcol[:, :], misc("bias")[:, 0:ROWS]).then_inc(bias_cols, 1)
            dve.tensor_copy(bcol_p[:, :], misc("bias")[:, 32:32 + ROWS]).then_inc(bias_cols, 1)
            dve.tensor_copy(c_col[:, :], misc("bias")[:, 64:64 + B]).then_inc(bias_cols, 1)
            dve.wait_ge(bias_cols, 3)
            dve.wait_ge(setup_ps, 2)
            for m, n, r in ((0, 6, R_SSQ), (6, 2, R_MOD + 3)):
                dve.tensor_tensor(mod[:, m:m + n, :], misc("mod")[:, B * m:B * (m + n)].rearrange("h (m b) -> h m b", b=B),
                                  bcol[:, r:r + n].unsqueeze(2).broadcast_to([H, n, B]), ALU.add).then_inc(mod_ready, 1)
            dve.wait_ge(mod_ready, 2)
            for m, n in ((0, 2), (5, 2)):
                dve.tensor_scalar(mod[:, m:m + 2 * n - 1:2, :], mod[:, m:m + 2 * n - 1:2, :], 1.0, None,
                                  ALU.add).then_inc(mod_ready, 1)

            def norm_input(g, n):
                b0, b1 = batches(g)
                return (cs, c_mv[:, b0:b1, :]) if n else (xs, x_mv)

            def norm_stats(g, n):
                s = layer(g)
                b0, b1 = batches(g)
                src, mv = norm_input(g, n)
                if s == CROSS0:
                    dve.wait_ge((x_in, c_in)[n][g], 16)
                if s in (SELF1, LAYERS) and n == 0:
                    dve.wait_ge(branch_added, B * (s - 1) + b1)
                if s == CROSS1 and n == 0:
                    dve.wait_ge(gated, 2 * b1)
                if (s, n) != (CROSS1, 1):
                    for j in range(PER):
                        stat(dve.bn_stats(stats[:, n, j, :], src[:, b0 + j, :]))
                    dve.wait_ge(stat_step, stat_steps[0])
                    for j in range(PER):
                        stat(dve.bn_aggr(mv[:, j, :], stats[:, n, j, :]))
                    dve.wait_ge(stat_step, stat_steps[0])
                stat(dve.tensor_scalar(var_eps[:, n, :], mv[:, :, 1], EPS[s], None, ALU.add))
                assert stat_steps[0] == stat_steps_to(g, n)

            def normalise(g, n):
                b0, b1 = batches(g)
                src, mv = norm_input(g, n)
                dve.wait_ge(rstd_ready, norms_to(g, n))
                if g >= 1:
                    dve.wait_ge(normed_ps, norms_to(g, n) - 1)
                for j in range(PER):
                    ins = dve.tensor_scalar(normed[:, n, j, :], src[:, b0 + j, :], mv[:, j, 0:1],
                                            rstd[:, n, j:j + 1], ALU.subtract, ALU.mult)
                ins.then_inc(normed_ready, 1)

            def leave_rest(g, n):
                dve.wait_ge(hi_ready, 2 * g + n + 1)
                r = (R_Q, R_K)[n][layer(g)]
                if g >= 1:
                    dve.wait_ge(split_ready, 2 * (2 * (g - 1) + n + 1))
                dve.scalar_tensor_tensor(out=rest[:, n, :], in0=misc("qk"[n], g), scalar=bcol_p[:, r:r + 1],
                                         in1=parts[:, n, 0, :], op0=ALU.add, op1=ALU.subtract).then_inc(rest_ready, 1)

            def row_max(u, c):
                dve.wait_ge(score_done, 2 * u + c + 1)
                if u >= 2 and c == 0:
                    dve.wait_ge(max_split, 2 * (u - 1))
                dve.tensor_reduce(neg_max[:, u % 2, :, CP * c:CP * (c + 1)],
                                  score_ps[:, :, :].rearrange("t e (a k) -> t e a k", k=T), AX.X, ALU.max,
                                  negate=True).then_inc(max_done, 1)

            def copy_max_rows(u):
                dve.wait_ge(max_ps, u + 1)
                if u >= 2:
                    max_rows_landed(dve, u - 2)
                dve.tensor_copy(max_rows[:, u % 2, :], misc("max", u)[0:2 * HEADS, 0:T // 2].bitcast(BF16)).then_inc(max_row_ready, 1)

            def divide(u):
                dve.wait_ge(turned_ps, u + 1)
                o = misc("out", u).rearrange("t (h d) -> t h d", d=QUAD)
                dve.reciprocal(r_sum[:, u % 2, :], o[:, :, D]).then_inc(sum_inv, 1)
                dve.wait_ge(sum_inv, u + 1)
                if u >= 2:
                    dve.wait_ge(attn_t_ps, u - 1)
                dve.tensor_tensor(attn[:, u % 2, :].rearrange("t (h d) -> t h d", d=D), o[:, :, 0:D],
                                  r_sum[:, u % 2, :].unsqueeze(2).broadcast_to([T, HEADS, D]),
                                  ALU.mult).then_inc(attn_ready, 1)

            def add_branch(u):
                s, b = u // B, u % B
                dve.wait_ge(proj_ps, u + 1)
                if s == SELF1:
                    if b >= 2:
                        dve.wait_ge(gated, 2 * (b - 1))
                    dve.tensor_tensor(branch[:, u % 2, :], misc("proj", u)[:, 0:H], b_out[:, 1, :], ALU.add).then_inc(branch_added, 1)
                else:
                    dve.wait_ge(x_bias_ready, b + 1 + (B if s == CROSS1 else 0))
                    dve.tensor_tensor(xs[:, b, :], misc("proj", u)[:, 0:H], x_bias[:, u % 2, :], ALU.add).then_inc(branch_added, 1)

            def copy_gates(b):
                dve.wait_ge(gate_ps, b + 1)
                if b == 0:
                    dve.wait_ge(loaded["bout"], 16 * 5)
                dve.tensor_tensor(gate[:, b, :, :].rearrange("t a h -> t (a h)"), misc("gate", b)[:, 0:2 * H],
                                  b_gate[:, :, :].rearrange("t a h -> t (a h)"), ALU.add).then_inc(gate_ready, 1)

            def add_mlp(q):
                dve.wait_ge(mlp_turned, q + 1)
                if q >= 2:
                    dve.wait_ge(x_final, q - 1)
                dve.tensor_tensor(mlp_out[:, q % 2, :].rearrange("t (j h) -> t j h", h=H),
                                  misc("mlp", q).rearrange("t (j h) -> t j h", h=H),
                                  gate[:, 4 * q:4 * q + 4, 1, :], ALU.mult).then_inc(mlp_gated, 1)
                dve.wait_ge(mlp_gated, q + 1)
                dve.tensor_tensor(xs[:, 4 * q:4 * q + 4, :].rearrange("t j h -> t (j h)"), mlp_out[:, q % 2, :],
                                  xs[:, 4 * q:4 * q + 4, :].rearrange("t j h -> t (j h)"), ALU.add).then_inc(x_final, 1)

            for tick in range(FIRST, LAST):
                g0, g1, g2, g3 = (front_at(tick, i) for i in range(4))
                norm = (g0, 0) if g0 is not None else (g1, 1) if (g1, 1) in NORMS else None
                if unit(tick + 2):
                    row_max(tick + 2, 0)
                if unit(tick + 1):
                    copy_max_rows(tick + 1)
                if norm:
                    norm_stats(*norm)
                if g3 is not None:
                    leave_rest(g3, 1)
                if unit(tick - 2):
                    add_branch(tick - 2)
                if unit(tick - 1):
                    divide(tick - 1)
                if unit(tick + 2):
                    row_max(tick + 2, 1)
                if norm:
                    normalise(*norm)
                if 0 <= tick < B:
                    copy_gates(tick)
                if tick == -3:
                    dve.tensor_copy(c_rep[:, :, :], c_col[:, :].unsqueeze(2).broadcast_to([H, B, 128])).then_inc(cond_rep, 1)
                if g2 is not None:
                    leave_rest(g2, 0)
                if 0 <= tick - MLP_TICK - 2 < 4:
                    add_mlp(tick - MLP_TICK - 2)

        @block.gpsimd
        def _(pool):
            pool.memset(ident[:, :], 0.0).then_inc(consts_ready, 1)
            pool.wait_ge(consts_ready, 1)
            pool.affine_select(out=ident[:, :], in_=ident[:, :], compare_op=ALU.not_equal, fill=1.0, base=0,
                               pattern=[[-1, 128]], channel_multiplier=1).then_inc(consts_ready, 1)
            pool.wait_ge(consts_ready, 2)
            pool.tensor_copy(ident_b[:, :], ident[:, :]).then_inc(consts_ready, 1)
            pool.memset(minus_half[:, :], -0.5).then_inc(consts_ready, 1)
            pool.wait_ge(loaded["brow"], 16 * 10)
            pool.tensor_copy(brow_p[:, :].rearrange("r (e d p) -> r e d p", e=2, d=D),
                             brow[:, :].rearrange("r (p e d) -> r e d p", e=2, d=D)).then_inc(rows_permuted, 1)

            def permute_weights(s):
                pool.wait_ge(loaded[("wA", "wB", "wC")[s]], (48, 32, 48)[s])
                for n, w in enumerate(((wq0[:, :], wkv0[:, 0:H]), (wqkv[:, 0:H], wqkv[:, H:2 * H]),
                                       (wqc[:, :], wkvc[:, 0:H]))[s]):
                    pool.tensor_copy(w_qk[:, s, n, :].rearrange("k (e d p) -> k e d p", e=2, d=D),
                                     w.rearrange("k (p e d) -> k e d p", e=2, d=D)).then_inc(w_permuted, 1)

            permute_weights(0)
            pool.memset(values[:, :, :, :, :], 0.0).then_inc(values_ones, 1)
            pool.wait_ge(values_ones, 1)
            pool.memset(values[:, :, :, :, D], 1.0).then_inc(values_ones, 1)

            def inverse_root(g, n):
                pool.wait_ge(stat_step, stat_steps_to(g, n))
                if g >= 1:
                    pool.wait_ge(normed_ready, norms_to(g, n) - 1)
                pool.tensor_tensor(rstd[:, n, :], var_eps[:, n, :], minus_half[:, :], ALU.pow).then_inc(rstd_ready, 1)

            def split_max(u):
                pool.wait_ge(max_done, 2 * (u + 1))
                if u >= 2:
                    pool.wait_ge(max_ps, u - 1)
                pool.tensor_copy(max_parts[:, u % 2, :, 0, :], neg_max[:, u % 2, :, :]).then_inc(max_split, 1)
                pool.wait_ge(max_split, 2 * u + 1)
                pool.tensor_tensor(max_parts[:, u % 2, :, 1, :], neg_max[:, u % 2, :, :], max_parts[:, u % 2, :, 0, :],
                                   ALU.subtract).then_inc(max_split, 1)

            def split_rest(g, n):
                m = 2 * g + n
                pool.wait_ge(rest_ready, m + 1)
                if g >= 1:
                    (q_in_place, k_in_place)[n](pool, g - 1)
                pool.tensor_copy(parts[:, n, 1, :], rest[:, n, :]).then_inc(split_ready, 1)
                pool.wait_ge(split_ready, 2 * m + 1)
                pool.tensor_tensor(parts[:, n, 2, :], rest[:, n, :], parts[:, n, 1, :], ALU.subtract).then_inc(split_ready, 1)

            def add_out_bias(u):
                s, b = u // B, u % B
                if u == 0:
                    pool.wait_ge(loaded["bout"], 16 * 5)
                if s == CROSS0 and b % 4 == 0:
                    pool.wait_ge(x_in[b // 4], 16)
                if s == CROSS1:
                    pool.wait_ge(gated, 2 * (b + 1))
                if u >= 2 and s == CROSS0 or s == CROSS1 and b >= 2:
                    pool.wait_ge(branch_added, u - 1)
                pool.tensor_tensor(x_bias[:, u % 2, :], xs[:, b, :], b_out[:, s, :], ALU.add).then_inc(x_bias_ready, 1)

            def add_gated(u):
                b = u - B
                pool.wait_ge(branch_added, u + 1)
                pool.wait_ge(gate_ready, b + 1)
                pool.tensor_tensor(branch[:, u % 2, :], branch[:, u % 2, :], gate[:, b, 0, :], ALU.mult).then_inc(gated, 1)
                pool.wait_ge(gated, 2 * b + 1)
                pool.tensor_tensor(xs[:, b, :], xs[:, b, :], branch[:, u % 2, :], ALU.add).then_inc(gated, 1)

            for tick in range(FIRST, LAST):
                g0, g1, g2, g3 = (front_at(tick, i) for i in range(4))
                norm = (g0, 0) if g0 is not None else (g1, 1) if (g1, 1) in NORMS else None
                if unit(tick - 3) and (tick - 3) // B == SELF1:
                    add_gated(tick - 3)
                if unit(tick - 2) and (tick - 2) // B != SELF1:
                    add_out_bias(tick - 2)
                if norm:
                    inverse_root(*norm)
                if g3 is not None:
                    split_rest(g3, 1)
                if unit(tick + 2):
                    split_max(tick + 2)
                if g2 is not None:
                    split_rest(g2, 0)
                if tick in (-4, -2):
                    permute_weights(3 + tick // 2)


_INS = ['x', 'ctx_1024', 'cond_1024', 'L0_xcond_Wq', 'L0_xcond_bq', 'L0_xcond_Wkv', 'L0_xcond_bkv', 'L0_xcond_Wp',
        'L0_xcond_bp', 'L0_xcond_Wss_q', 'L0_xcond_bss_q', 'L0_xcond_Wss_kv', 'L0_xcond_bss_kv', 'L1_xcond_W_mod',
        'L1_xcond_b_mod', 'L1_xcond_W_qkv', 'L1_xcond_b_qkv', 'L1_xcond_W_proj', 'L1_xcond_b_proj', 'L1_xcond_W_qc',
        'L1_xcond_b_qc', 'L1_xcond_W_kvc', 'L1_xcond_b_kvc', 'L1_xcond_W_cproj', 'L1_xcond_b_cproj',
        'L1_xcond_W_mlp1', 'L1_xcond_b_mlp1', 'L1_xcond_W_mlp2', 'L1_xcond_b_mlp2']
_OUTS = [((16, 128, 128), 'float32')]


def kernel(**inputs):
    import numpy as _np
    import concourse.bacc as _bacc
    from concourse import mybir as _mybir
    from concourse.bass_utils import run_bass_kernel_spmd as _run

    nc = _bacc.Bacc("TRN2", target_bir_lowering=False, num_devices=1)
    arrays, args = {}, []
    for name in _INS:
        a = _np.ascontiguousarray(inputs[name])
        arrays[f"in_{name}_dram"] = a
        args.append(nc.dram_tensor(f"in_{name}_dram", a.shape, _mybir.dt.from_np(a.dtype), kind="ExternalInput").ap())
    for i, (shape, dtype) in enumerate(_OUTS):
        dt = _mybir.dt.from_np(_np.dtype(dtype))
        args.append(nc.dram_tensor(f"out_{i}_dram", shape, dt, kind="ExternalOutput").ap())
    build(nc, *args)
    r = _run(nc, [arrays], core_ids=[0])
    got = tuple(r.results[0][f"out_{i}_dram"] for i in range(len(_OUTS)))
    return got[0]
```
